# Optimizing a Trainium2 kernel written in Bass

```python
import numpy as np
import jax
import jax.numpy as jnp

def _softmax(x, axis=-1):
    return jax.nn.softmax(x, axis=axis)

def _gelu(x):
    return jax.nn.gelu(x, approximate=True)

def _silu(x):
    return jax.nn.silu(x)

def _sigmoid(x):
    return jax.nn.sigmoid(x)

def _layernorm(x, axis=-1, eps=1e-05):
    m = jnp.mean(x, axis=axis, keepdims=True)
    v = jnp.var(x, axis=axis, keepdims=True)
    return (x - m) / jnp.sqrt(v + eps)

def _scatter_add(tgt, idx, src, axis=0):
    return tgt.at[idx].add(src)

def _segment_sum(src, seg, n):
    return jax.ops.segment_sum(src, seg, n)
kernel_name = 'mk_macaron_d2_jaxref_r8_de271d'

def setup_inputs(seed: int=0):
    np.random.seed(seed)
    _w = jnp.asarray

    def _L0_attn_setup():
        import math
        import jax, jax.numpy as jnp
        import numpy as np
        B, S, D, H = (2, 256, 256, 16)
        HD = D // H
        ROPE_BASE = 10000.0

        def _rope_cos_sin(seqlen, dim):
            inv_freq = 1.0 / ROPE_BASE ** (jnp.arange(0, dim, 2, dtype=jnp.float32) / dim)
            t = jnp.arange(seqlen, dtype=jnp.float32)
            freqs = jnp.outer(t, inv_freq)
            return (jnp.cos(freqs), jnp.sin(freqs))
        key = jax.random.key(seed)
        k0, k1, k2 = jax.random.split(key, 3)
        return {'x': jax.random.normal(k0, (B, S, D), dtype=jnp.float32), 'Wqkv': jax.random.normal(k1, (D, 3 * D), dtype=jnp.float32) * 0.02, 'bqkv': jnp.zeros((3 * D,), dtype=jnp.float32), 'Wout': jax.random.normal(k2, (D, D), dtype=jnp.float32) * 0.02, 'bout': jnp.zeros((D,), dtype=jnp.float32)}
    _L0_attn_in = _L0_attn_setup()

    def _L0_ffn_setup():
        import jax, jax.numpy as jnp
        import numpy as np
        NUM_EXPERTS = 8
        TOP_K = 2
        key = jax.random.key(seed)
        ks = jax.random.split(key, 7)
        B, S, H, I, E = (4, 256, 256, 256, NUM_EXPERTS)
        sc = 0.02
        return {'hidden_states': jax.random.normal(ks[0], (B, S, H), dtype=jnp.float32), 'gate_w': jax.random.normal(ks[1], (E, H), dtype=jnp.float32) * sc, 'gate_b': jax.random.normal(ks[2], (E,), dtype=jnp.float32) * sc, 'w1': jax.random.normal(ks[3], (E, 2 * I, H), dtype=jnp.float32) * sc, 'b1': jax.random.normal(ks[4], (E, 2 * I), dtype=jnp.float32) * sc, 'w2': jax.random.normal(ks[5], (E, H, I), dtype=jnp.float32) * sc, 'b2': jax.random.normal(ks[6], (E, H), dtype=jnp.float32) * sc}
    _L0_ffn_in = _L0_ffn_setup()

    def _L1_attn_setup():
        import math
        import jax, jax.numpy as jnp
        import numpy as np
        HID = 256
        H = 16
        HKV = 8
        D = HID // H
        F = D
        SEQ = 256
        BATCH = 2
        THETA = 10000.0

        def _rotate_half(x):
            x1, x2 = (x[..., :x.shape[-1] // 2], x[..., x.shape[-1] // 2:])
            return jnp.concatenate((-x2, x1), axis=-1)

        def _softmax_kernel(x, R):
            n = jnp.sqrt(jnp.sum(x * x, axis=-1, keepdims=True))
            x = x / jnp.maximum(n, 1e-06)
            p = jnp.einsum('...d,ed->...e', x, R)
            feats = jnp.concatenate([jnp.sin(p), jnp.cos(p)], axis=-1)
            return feats / math.sqrt(F)
        key = jax.random.key(seed)
        ks = jax.random.split(key, 10)
        s = lambda k, shape, scale=0.02: jax.random.normal(k, shape, dtype=jnp.float32) * scale
        return {'hidden_states': jax.random.normal(ks[0], (BATCH, SEQ, HID), dtype=jnp.float32), 'Wq': s(ks[1], (HID, HID)), 'bq': s(ks[2], (HID,)), 'Wk': s(ks[3], (HKV * D, HID)), 'bk': s(ks[4], (HKV * D,)), 'Wv': s(ks[5], (HKV * D, HID)), 'bv': s(ks[6], (HKV * D,)), 'Wo': s(ks[7], (HID, HID)), 'bo': s(ks[8], (HID,)), 'rand_matrix': jax.random.normal(ks[9], (F // 2, D), dtype=jnp.float32)}
    _L1_attn_in = _L1_attn_setup()

    def _L1_ffn_setup():
        import jax, jax.numpy as jnp
        import numpy as np
        B, S, D, H = (4, 256, 256, 1024)

        def fwht(x):
            orig_shape = x.shape
            n = orig_shape[-1]
            x = x.reshape(-1, n)
            h = 1
            while h < n:
                xb = x.reshape(-1, n // (2 * h), 2, h)
                a = xb[:, :, 0, :]
                b = xb[:, :, 1, :]
                x = jnp.stack([a + b, a - b], axis=2).reshape(-1, n)
                h *= 2
            scale = jnp.asarray(1.0 / np.sqrt(n), dtype=x.dtype)
            return (x * scale).reshape(orig_shape)
        key = jax.random.key(seed)
        kx, k1, k2, k3 = jax.random.split(key, 4)
        x = jax.random.normal(kx, (B, S, D), dtype=jnp.float32)
        W1 = jax.random.normal(k1, (H, D), dtype=jnp.float32) * (1.0 / np.sqrt(D))
        W2 = jax.random.normal(k2, (D, H), dtype=jnp.float32) * (1.0 / np.sqrt(H))
        W3 = jax.random.normal(k3, (H, D), dtype=jnp.float32) * (1.0 / np.sqrt(D))
        return {'x': x, 'W1': W1, 'W2': W2, 'W3': W3}
    _L1_ffn_in = _L1_ffn_setup()
    _d = {'L0_attn_x': _L0_attn_in['x'], 'L0_attn_Wqkv': _L0_attn_in['Wqkv'], 'L0_attn_bqkv': _L0_attn_in['bqkv'], 'L0_attn_Wout': _L0_attn_in['Wout'], 'L0_attn_bout': _L0_attn_in['bout'], 'L0_ffn_gate_w': _L0_ffn_in['gate_w'], 'L0_ffn_gate_b': _L0_ffn_in['gate_b'], 'L0_ffn_w1': _L0_ffn_in['w1'], 'L0_ffn_b1': _L0_ffn_in['b1'], 'L0_ffn_w2': _L0_ffn_in['w2'], 'L0_ffn_b2': _L0_ffn_in['b2'], 'L1_attn_Wq': _L1_attn_in['Wq'], 'L1_attn_bq': _L1_attn_in['bq'], 'L1_attn_Wk': _L1_attn_in['Wk'], 'L1_attn_bk': _L1_attn_in['bk'], 'L1_attn_Wv': _L1_attn_in['Wv'], 'L1_attn_bv': _L1_attn_in['bv'], 'L1_attn_Wo': _L1_attn_in['Wo'], 'L1_attn_bo': _L1_attn_in['bo'], 'L1_attn_rand_matrix': _L1_attn_in['rand_matrix'], 'L1_ffn_W1': _L1_ffn_in['W1'], 'L1_ffn_W2': _L1_ffn_in['W2'], 'L1_ffn_W3': _L1_ffn_in['W3']}
    _x0 = _d['L0_attn_x']
    _d['L0_attn_x'] = jax.random.normal(jax.random.fold_in(jax.random.key(seed), 1), (4, 512, 256), dtype=_x0.dtype)
    del _x0
    return _d

def reference(L0_attn_x, L0_attn_Wqkv, L0_attn_bqkv, L0_attn_Wout, L0_attn_bout, L0_ffn_gate_w, L0_ffn_gate_b, L0_ffn_w1, L0_ffn_b1, L0_ffn_w2, L0_ffn_b2, L1_attn_Wq, L1_attn_bq, L1_attn_Wk, L1_attn_bk, L1_attn_Wv, L1_attn_bv, L1_attn_Wo, L1_attn_bo, L1_attn_rand_matrix, L1_ffn_W1, L1_ffn_W2, L1_ffn_W3):

    def _L0_attn_ref(x, Wqkv, bqkv, Wout, bout):
        import math
        import jax, jax.numpy as jnp
        import numpy as np
        B, S, D, H = (2, 256, 256, 16)
        HD = D // H
        ROPE_BASE = 10000.0

        def _rope_cos_sin(seqlen, dim):
            inv_freq = 1.0 / ROPE_BASE ** (jnp.arange(0, dim, 2, dtype=jnp.float32) / dim)
            t = jnp.arange(seqlen, dtype=jnp.float32)
            freqs = jnp.outer(t, inv_freq)
            return (jnp.cos(freqs), jnp.sin(freqs))
        b, s, d = x.shape
        hd = d // H
        qkv = (x @ Wqkv + bqkv).reshape(b, s, 3, H, hd)
        q, k, v = (qkv[:, :, 0], qkv[:, :, 1], qkv[:, :, 2])
        cos, sin = _rope_cos_sin(s, hd)
        c = cos[:, None, :]
        si = sin[:, None, :]

        def rot(t):
            t1, t2 = jnp.split(t.astype(jnp.float32), 2, axis=-1)
            return jnp.concatenate([t1 * c - t2 * si, t1 * si + t2 * c], axis=-1).astype(x.dtype)
        q = rot(q)
        k = rot(k)
        scale = 1.0 / math.sqrt(hd)
        scores = jnp.einsum('bthd,bshd->bhts', q, k * scale)
        causal_mask = jnp.triu(jnp.full((s, s), -10000.0, dtype=scores.dtype), 1)
        attn = jax.nn.softmax(scores + causal_mask, axis=-1)
        ctx = jnp.einsum('bhts,bshd->bthd', attn, v).reshape(b, s, d)
        return ctx @ Wout + bout

    def _L0_ffn_ref(hidden_states, gate_w, gate_b, w1, b1, w2, b2):
        import jax, jax.numpy as jnp
        import numpy as np
        NUM_EXPERTS = 8
        TOP_K = 2
        B, S, H = hidden_states.shape
        x = hidden_states.reshape(-1, H)
        logits = x @ gate_w.T + gate_b
        top_vals, top_idx = jax.lax.top_k(logits, TOP_K)
        routing = jax.nn.softmax(top_vals.astype(jnp.float32), axis=-1).astype(x.dtype)
        out = jnp.zeros_like(x)
        E = w1.shape[0]
        for e in range(E):
            h = x @ w1[e].T + b1[e]
            x_glu = h[:, 0::2]
            x_lin = h[:, 1::2]
            y = x_glu * jax.nn.sigmoid(1.702 * x_glu) * (x_lin + 1.0)
            ye = y @ w2[e].T + b2[e]
            we = jnp.sum(routing * (top_idx == e), axis=-1)
            out = out + ye * we[:, None]
        return out.reshape(B, S, H)

    def _L1_attn_ref(hidden_states, Wq, bq, Wk, bk, Wv, bv, Wo, bo, rand_matrix):
        import math
        import jax, jax.numpy as jnp
        import numpy as np
        HID = 256
        H = 16
        HKV = 8
        D = HID // H
        F = D
        SEQ = 256
        BATCH = 2
        THETA = 10000.0

        def _rotate_half(x):
            x1, x2 = (x[..., :x.shape[-1] // 2], x[..., x.shape[-1] // 2:])
            return jnp.concatenate((-x2, x1), axis=-1)

        def _softmax_kernel(x, R):
            n = jnp.sqrt(jnp.sum(x * x, axis=-1, keepdims=True))
            x = x / jnp.maximum(n, 1e-06)
            p = jnp.einsum('...d,ed->...e', x, R)
            feats = jnp.concatenate([jnp.sin(p), jnp.cos(p)], axis=-1)
            return feats / math.sqrt(F)
        b, s, _ = hidden_states.shape
        q = (hidden_states @ Wq.T + bq).reshape(b, s, H, D).transpose(0, 2, 1, 3)
        k = (hidden_states @ Wk.T + bk).reshape(b, s, HKV, D).transpose(0, 2, 1, 3)
        v = (hidden_states @ Wv.T + bv).reshape(b, s, HKV, D).transpose(0, 2, 1, 3)
        inv_freq = 1.0 / THETA ** (jnp.arange(0, D, 2, dtype=jnp.float32) / D)
        freqs = jnp.arange(s, dtype=jnp.float32)[:, None] * inv_freq[None, :]
        emb = jnp.concatenate((freqs, freqs), axis=-1)
        cos = jnp.cos(emb)[None, None, :, :]
        sin = jnp.sin(emb)[None, None, :, :]
        q = q * cos + _rotate_half(q) * sin
        k = k * cos + _rotate_half(k) * sin
        rep = H // HKV
        k = jnp.repeat(k, rep, axis=1)
        v = jnp.repeat(v, rep, axis=1)
        qp = _softmax_kernel(q, rand_matrix)
        kp = _softmax_kernel(k, rand_matrix)
        kv = jnp.einsum('bhsf,bhsd->bsfd', kp, v)
        out = jnp.einsum('bhsf,bsfd->bhsd', qp, kv)
        out = out.reshape(b, s, HID)
        return out @ Wo.T + bo

    def _L1_ffn_ref(x, W1, W2, W3):
        import jax, jax.numpy as jnp
        import numpy as np
        B, S, D, H = (4, 256, 256, 1024)

        def fwht(x):
            orig_shape = x.shape
            n = orig_shape[-1]
            x = x.reshape(-1, n)
            h = 1
            while h < n:
                xb = x.reshape(-1, n // (2 * h), 2, h)
                a = xb[:, :, 0, :]
                b = xb[:, :, 1, :]
                x = jnp.stack([a + b, a - b], axis=2).reshape(-1, n)
                h *= 2
            scale = jnp.asarray(1.0 / np.sqrt(n), dtype=x.dtype)
            return (x * scale).reshape(orig_shape)
        up_gate = jnp.einsum('bsd,hd->bsh', x, W1)
        up_lin = jnp.einsum('bsd,hd->bsh', x, W3)
        hidden = jax.nn.silu(up_gate) * up_lin
        hidden = fwht(hidden)
        out = jnp.einsum('bsh,dh->bsd', hidden, W2)
        return out
    x = L0_attn_x
    x = x + 0.5 * _L0_ffn_ref(_layernorm(x, axis=-1), L0_ffn_gate_w, L0_ffn_gate_b, L0_ffn_w1, L0_ffn_b1, L0_ffn_w2, L0_ffn_b2)
    x = x + _L0_attn_ref(_layernorm(x, axis=-1), L0_attn_Wqkv, L0_attn_bqkv, L0_attn_Wout, L0_attn_bout)
    x = x + 0.5 * _L0_ffn_ref(_layernorm(x, axis=-1), L0_ffn_gate_w, L0_ffn_gate_b, L0_ffn_w1, L0_ffn_b1, L0_ffn_w2, L0_ffn_b2)
    x = x + 0.5 * _L1_ffn_ref(_layernorm(x, axis=-1), L1_ffn_W1, L1_ffn_W2, L1_ffn_W3)
    x = x + _L1_attn_ref(_layernorm(x, axis=-1), L1_attn_Wq, L1_attn_bq, L1_attn_Wk, L1_attn_bk, L1_attn_Wv, L1_attn_bv, L1_attn_Wo, L1_attn_bo, L1_attn_rand_matrix)
    x = x + 0.5 * _L1_ffn_ref(_layernorm(x, axis=-1), L1_ffn_W1, L1_ffn_W2, L1_ffn_W3)
    return x

_drawn_inputs = setup_inputs


def setup_inputs(seed=0):
    import zlib

    import numpy as np

    out = dict(_drawn_inputs(seed))
    spreads = {'L0_attn_bqkv': (0.0, 0.1), 'L0_attn_bout': (0.0, 0.1)}
    factors = {'L0_attn_Wqkv': 4.117,
     'L0_ffn_gate_b': 7.598,
     'L0_ffn_b1': 8.0,
     'L0_ffn_b2': 3.501,
     'L1_attn_bq': 8.0,
     'L1_attn_bk': 8.0,
     'L1_attn_bv': 8.0,
     'L1_attn_bo': 3.24}
    for name, (base, spread) in spreads.items():
        noise = np.random.default_rng([zlib.crc32(name.encode()), seed]).standard_normal(out[name].shape)
        drawn = base * np.exp(spread * noise) if base else spread * noise
        out[name] = jnp.asarray(drawn.astype(out[name].dtype))
    for name, factor in factors.items():
        out[name] = (out[name] * factor).astype(out[name].dtype)
    return out
```

```python
from contextlib import ExitStack

import numpy as np
import concourse.bass as bass
from concourse import mybir

ALU = mybir.AluOpType
ACT = mybir.ActivationFunctionType
F32 = mybir.dt.float32
F32R = mybir.dt.float32r
U32 = mybir.dt.uint32
AX_X = mybir.AxisListType.X

P = 128
BATCH, SEQ, D = 4, 512, 256
TOKENS = BATCH * SEQ
TILES = TOKENS // P
BATCH_P = P // BATCH
BT = SEQ // P
KC = D // P
EPS = 1e-5

E, I = 8, 256
IC = I // P
HID = 1024
HC = HID // P
H, HD = 16, 16
HALF = HD // 2
HKV = 8
MASK = -10000.0

REC_W1 = KC * 2 * I
REC_W2 = IC * D
REC = REC_W1 + REC_W2 + 2 * IC


def f32(ap):
    return ap.bitcast(F32)


class Shared:
    pass


class Weights:

    def __init__(self, hi, lo, out_hi, out_lo):
        self.hi, self.lo, self.out_hi, self.out_lo = hi, lo, out_hi, out_lo


class Biases:

    def __init__(self, sig, scale, gate, lin):
        self.sig, self.scale, self.gate, self.lin = sig, scale, gate, lin


class Semaphores:

    def __init__(self, nc, ctx, tag):
        self.nc, self.tag, self.held = nc, tag, []
        ctx.callback(self.clear)

    def __call__(self, name):
        self.held.append(self.nc.alloc_semaphore(name=f"{self.tag}_{name}"))
        return self.held[-1]

    def clear(self):
        self.nc.clear_and_free_semaphores(self.held)
        self.nc.all_engine_barrier()


class Norm:

    def __init__(self, nc, sem, g, tag, slots):
        self.nc, self.g, self.slots = nc, g, slots
        s = lambda n: sem(f"{tag}_{n}")
        self.stats_done = s("stats_done")
        self.var_done = s("var_done")
        self.eps_done = s("eps_done")
        self.rstd_done = s("rstd_done")
        self.xn_done = s("xn_done")
        self.turned = s("turned")
        self.hi_done = s("hi_done")
        self.lo_done = s("lo_done")

    def slot(self, b):
        return b % self.slots if isinstance(b, int) else 0

    def stats(self, dve, b, x_block):
        nc, g, q = self.nc, self.g, self.slot(b)
        for i in range(BT):
            last = nc.vector.bn_stats(g.bn6[:, q, i, :], x_block(i))
        last.then_inc(self.stats_done, 1)
        dve.wait_ge(self.stats_done, 1)
        dve.wait_ge(self.stats_done, b + 1)
        for i in range(BT):
            last = nc.vector.bn_aggr(g.bn2[:, q, i, :], g.bn6[:, q, i, :])
        last.then_inc(self.var_done, 1)

    def rstd(self, pool, b):
        nc, g, q = self.nc, self.g, self.slot(b)
        pool.wait_ge(self.var_done, b + 1)
        nc.gpsimd.tensor_tensor(g.var_eps[:, q, :], g.bn2[:, q, :, 1], g.eps[:, 0:BT], ALU.add) \
            .then_inc(self.eps_done, 1)
        pool.wait_ge(self.eps_done, b + 1)
        nc.gpsimd.tensor_tensor(g.rstd[:, q, :], g.var_eps[:, q, :], g.neg_half[:, 0:BT], ALU.pow) \
            .then_inc(self.rstd_done, 1)

    def normalise(self, dve, b, x_block):
        nc, g, q = self.nc, self.g, self.slot(b)
        dve.wait_ge(self.rstd_done, b + 1)
        if not isinstance(b, int) or b >= self.slots:
            dve.wait_ge(self.turned, b - self.slots + 1)
        for i in range(BT):
            last = nc.vector.tensor_scalar(g.xn[:, q, i, :], x_block(i), g.bn2[:, q, i, 0:1],
                                           g.rstd[:, q, i:i + 1], ALU.subtract, ALU.mult)
        last.then_inc(self.xn_done, 1)

    def turn(self, pe, b, banks):
        nc, g, q = self.nc, self.g, self.slot(b)
        pe.wait_ge(self.xn_done, b + 1)
        if not isinstance(b, int) or b >= self.slots:
            pe.wait_ge(self.lo_done, b - self.slots + 1)
        for k in range(KC):
            for i in range(BT):
                last = nc.tensor.transpose(g.ps[:, banks + k, i * P:(i + 1) * P],
                                           g.xn[:, q, i, k * P:(k + 1) * P], g.ident[:, :])
        last.then_inc(self.turned, 1)

    def high(self, act, b, banks, xt_hi):
        act.wait_ge(self.turned, b + 1)
        self.nc.scalar.activation(xt_hi, self.g.ps[:, banks:banks + KC, :], ACT.Copy) \
            .then_inc(self.hi_done, 1)

    def low(self, dve, b, banks, xt_hi, xt_lo):
        dve.wait_ge(self.hi_done, b + 1)
        self.nc.vector.tensor_tensor(xt_lo, self.g.ps[:, banks:banks + KC, :], f32(xt_hi),
                                     ALU.subtract).then_inc(self.lo_done, 1)


class Gated:

    def __init__(self, nc, sem, g, tag, units, period, group, slots, before_first, weights, rhs,
                 biases, scale, xr):
        self.nc, self.g, self.before_first = nc, g, before_first
        self.units, self.period, self.group, self.slots = units, period, group, slots
        self.weights, self.rhs, self.biases, self.scale, self.xr = weights, rhs, biases, scale, xr
        s = lambda n: sem(f"{tag}_{n}")
        self.gl_ready = s("gl_ready")
        self.sig_ready = s("sig_ready")
        self.gate_done = s("gate_done")
        self.y_done = s("y_done")
        self.yhi_ready = s("yhi_ready")
        self.ylo_ready = s("ylo_ready")
        self.y_free = s("y_free")
        self.out_added = s("out_added")
        self.lag = group + 1

    def first(self, pe, n0, it):
        nc, g = self.nc, self.g
        n = n0 + it * self.period
        if n0 >= 2:
            pe.wait_ge(self.y_done, n - 1)
        w = self.weights(n0)
        self.before_first(pe, n0, it)
        for half in range(2):
            bank = g.ps[:, 2 * (n0 % 2) + half, :]
            steps = [(w.hi, 0), (w.hi, 1), (w.lo, 0)]
            for k in range(KC):
                for q, (part, low) in enumerate(steps):
                    last = nc.tensor.matmul(bank, part(k, half), self.rhs(n0, it, k, low),
                                            start=(k == 0 and q == 0), stop=(k == KC - 1 and q == 2))
        last.then_inc(self.gl_ready, 1)

    def second(self, pe, n0, it):
        nc, g = self.nc, self.g
        n = n0 + it * self.period
        m0, c = n0 // self.group, n0 % self.group
        m = m0 + it * (self.period // self.group)
        if c == 0 and m0 >= self.slots:
            pe.wait_ge(self.out_added, m - self.slots + 1)
        pe.wait_ge(self.ylo_ready, n + 1)
        w = self.weights(n0)
        for i in range(BT):
            bank = 4 + 2 * (m0 % self.slots) + i // 2
            out = g.ps[:, bank, (i % 2) * D:(i % 2 + 1) * D]
            yhi = g.yhi[:, n0 % 4, i * P:(i + 1) * P]
            ylo = g.ylo[:, n0 % 4, i * P:(i + 1) * P]
            for q, (a, b) in enumerate([(yhi, w.out_hi), (yhi, w.out_lo), (ylo, w.out_hi)]):
                last = nc.tensor.matmul(out, a, b, start=(c == 0 and q == 0 and i % 2 == 0),
                                        stop=(c == self.group - 1 and q == 2), skip_group_check=True)
        last.then_inc(self.y_free, 1)

    def sigmoid(self, act, n0, it):
        nc, g = self.nc, self.g
        n = n0 + it * self.period
        act.wait_ge(self.gl_ready, n + 1)
        if n0 >= 2:
            act.wait_ge(self.gate_done, n - 1)
        b = self.biases(n0)
        nc.scalar.activation(g.sig[:, n0 % 2, :], g.ps[:, 2 * (n0 % 2), :], ACT.Sigmoid,
                             bias=b.sig, scale=b.scale).then_inc(self.sig_ready, 1)

    def high(self, act, n0, it):
        nc, g = self.nc, self.g
        n = n0 + it * self.period
        act.wait_ge(self.y_done, n + 1)
        act.wait_ge(self.y_free, n + 1)
        nc.scalar.activation(g.yhi[:, n0 % 4, :], g.y[:, n0 % 2, :], ACT.Copy) \
            .then_inc(self.yhi_ready, 1)

    def gate(self, dve, n0, it):
        nc, g = self.nc, self.g
        n = n0 + it * self.period
        dve.wait_ge(self.sig_ready, n + 1)
        b = self.biases(n0)
        nc.vector.scalar_tensor_tensor(out=g.gated[:, n0 % 2, :], in0=g.ps[:, 2 * (n0 % 2), :],
                                       scalar=b.gate, in1=g.sig[:, n0 % 2, :],
                                       op0=ALU.add, op1=ALU.mult).then_inc(self.gate_done, 1)

    def product(self, dve, n0, it):
        nc, g = self.nc, self.g
        n = n0 + it * self.period
        dve.wait_ge(self.gate_done, n + 1)
        b = self.biases(n0)
        nc.vector.scalar_tensor_tensor(out=g.y[:, n0 % 2, :], in0=g.ps[:, 2 * (n0 % 2) + 1, :],
                                       scalar=b.lin, in1=g.gated[:, n0 % 2, :],
                                       op0=ALU.add, op1=ALU.mult).then_inc(self.y_done, 1)

    def low(self, dve, n0, it):
        nc, g = self.nc, self.g
        n = n0 + it * self.period
        dve.wait_ge(self.yhi_ready, n + 1)
        nc.vector.tensor_tensor(g.ylo[:, n0 % 4, :], g.y[:, n0 % 2, :], f32(g.yhi[:, n0 % 4, :]),
                                ALU.subtract).then_inc(self.ylo_ready, 1)

    def add(self, dve, m0, it):
        nc, g = self.nc, self.g
        m = m0 + it * (self.period // self.group)
        dve.wait_ge(self.y_free, 4 + self.group * (m + 1))
        dve.wait_ge(self.out_added, m)
        for i in range(BT):
            bank = 4 + 2 * (m0 % self.slots) + i // 2
            x = self.xr(m0, it, i)
            last = nc.vector.scalar_tensor_tensor(
                out=x, in0=g.ps[:, bank, (i % 2) * D:(i % 2 + 1) * D], scalar=self.scale(m0, it, i),
                in1=x, op0=ALU.mult, op1=ALU.add)
        last.then_inc(self.out_added, 1)

    def spans(self, shift):
        trips = (self.units - shift) // self.period
        if (self.units - shift) % self.period == 0:
            trips -= 1
        return range(shift), trips, range(shift, shift + self.period), \
            range(shift + trips * self.period, self.units)

    def run(self, eng, step, shift):
        before, trips, body, after = self.spans(shift)
        for n in before:
            step(n, 0)
        with eng.Fori(0, trips) as it:
            for n in body:
                step(n, it)
        for n in after:
            step(n, 0)

    def run_pe(self, pe):
        pe.sem_inc(self.y_free, 4)
        self.first(pe, 0, 0)
        self.first(pe, 1, 0)

        def step(n, it):
            if n + 2 < self.units:
                self.first(pe, n + 2, it)
            self.second(pe, n, it)
        self.run(pe, step, self.slots * self.group)

    def run_act(self, act):
        self.sigmoid(act, 0, 0)

        def step(n, it):
            if n + 1 < self.units:
                self.sigmoid(act, n + 1, it)
            self.high(act, n, it)
        self.run(act, step, self.period)

    def run_dve(self, dve):
        self.gate(dve, 0, 0)
        self.product(dve, 0, 0)

        def step(n, it):
            if n + 1 < self.units:
                self.gate(dve, n + 1, it)
            self.low(dve, n, it)
            if n + 1 < self.units:
                self.product(dve, n + 1, it)
            if n >= self.lag and (n - self.lag) % self.group == 0:
                self.add(dve, (n - self.lag) // self.group, it)
        self.run(dve, step, self.lag)
        done = (self.units - 1 - self.lag) // self.group + 1
        for m in range(done, self.units // self.group):
            self.add(dve, m, 0)


def split_weights(nc, pool, done, at, hi, lo, raw):
    nc.gpsimd.tensor_copy(hi, raw).then_inc(done, 1)
    pool.wait_ge(done, at + 1)
    nc.gpsimd.tensor_tensor(lo, raw, f32(hi), ALU.subtract).then_inc(done, 1)
    return at + 2


def program(nc, ins, out, stages=6):
    with ExitStack() as ctx:
        sb = lambda n, shape, dt=F32: ctx.enter_context(nc.sbuf_tensor(n, shape, dt))
        sem = lambda n: ctx.enter_context(nc.semaphore(n))
        g = Shared()
        g.ps = ctx.enter_context(nc.psum_tensor("ps", [P, 8, 512], F32))
        g.x = sb("x", [P, TILES, D])
        g.turned_dram = [nc.dram_tensor(f"x_turned{n}", (TOKENS, D), F32, kind="Internal").ap() for n in range(2)]
        g.ident = sb("ident", [P, P])
        g.neg_half = sb("neg_half", [P, 64])
        g.eps = sb("eps", [P, 64])
        g.bn6 = sb("bn6", [P, 2, BT, 6])
        g.bn2 = sb("bn2", [P, 2, BT, 2])
        g.var_eps = sb("var_eps", [P, 2, BT])
        g.rstd = sb("rstd", [P, 2, BT])
        g.wqkv = [sb(f"wqkv{q}", [P, KC, 3 * D], F32R) for q in range(2)]
        g.wout = [sb(f"wout{q}", [P, KC, D], F32R) for q in range(2)]
        g.lqkv = [sb(f"lqkv{q}", [P, KC, 2 * D], F32R) for q in range(2)]
        g.lout = [sb(f"lout{q}", [P, KC, D], F32R) for q in range(2)]
        g.w1 = [sb(f"w1_{q}", [P, KC, HID], F32R) for q in range(2)]
        g.w3 = [sb(f"w3_{q}", [P, KC, HID], F32R) for q in range(2)]
        g.w2 = [sb(f"w2_{q}", [P, HC, D], F32R) for q in range(2)]
        x_dram = ins["x"].rearrange("b (t p) d -> p (b t) d", p=P)

        experts_stage(nc, g, ins, 0, x_dram)
        if stages > 1:
            attention_stage(nc, g, ins)
        if stages > 2:
            experts_stage(nc, g, ins, 1, None)
        if stages > 3:
            hadamard_stage(nc, g, ins, 0)
        if stages > 4:
            features_stage(nc, g, ins)
        if stages > 5:
            hadamard_stage(nc, g, ins, 1)
        stored = sem("stored")
        block = ctx.enter_context(nc.Block())

        @block.sync
        def _(sp):
            rows = out.rearrange("b s d -> (b s) d")
            for b in range(BATCH):
                at = slice(b * BATCH_P, (b + 1) * BATCH_P)
                if stages > 4:
                    sp.dma_start(by_heads(rows, b), g.x[at, :, :]).then_inc(stored, 16)
                elif stages > 1:
                    sp.dma_start(by_sixteens(rows)[at], g.x[at, :, :]).then_inc(stored, 16)
                else:
                    sp.dma_start(by_tiles(rows, b), g.x[:, b * BT:(b + 1) * BT, :]).then_inc(stored, 16)
            sp.wait_ge(stored, 16 * BATCH)


def by_tiles(rows, b):
    return rows.rearrange("(t p) d -> p t d", p=P)[:, b * BT:(b + 1) * BT, :]


def by_sixteens(rows):
    return rows.rearrange("(p a) d -> p a d", a=TILES)


def by_heads(rows, b):
    return rows[b * SEQ:(b + 1) * SEQ, :].rearrange("(h q) d -> q h d", h=TILES)


def x_of(g):
    return lambda b: (lambda i: g.x[:, b * BT + i, :])


def gated_buffers(g, sb):
    g.xn = sb("xn", [P, 2, BT, D])
    g.xt = [sb(f"xt{q}", [P, KC, TOKENS], F32R) for q in range(2)]
    g.sig = sb("sig", [P, 2, 512])
    g.gated = sb("gated", [P, 2, 512])
    g.y = sb("y", [P, 2, 512])
    g.yhi = sb("yhi", [P, 4, 512], F32R)
    g.ylo = sb("ylo", [P, 4, 512], F32R)


def norm_pe(norm, pe):
    for b in range(BATCH):
        norm.turn(pe, b, 4 + 2 * (b % 2))


def norm_act(norm, act, xt):
    for b in range(BATCH):
        norm.high(act, b, 4 + 2 * (b % 2), xt[0][:, :, b * SEQ:(b + 1) * SEQ])


def norm_dve(norm, dve, xt, x_block, arrived=None):
    def low(b):
        norm.low(dve, b, 4 + 2 * (b % 2), xt[0][:, :, b * SEQ:(b + 1) * SEQ],
                 xt[1][:, :, b * SEQ:(b + 1) * SEQ])
    for b in range(BATCH):
        if arrived is not None:
            dve.wait_ge(arrived[b], 16)
        norm.stats(dve, b, x_block(b))
        norm.normalise(dve, b, x_block(b))
        if b:
            low(b - 1)
    low(BATCH - 1)


def experts_stage(nc, g, ins, which, x_dram):
    with ExitStack() as ctx:
        tag = f"moe{which}"
        sb = lambda n, shape, dt=F32: ctx.enter_context(nc.sbuf_tensor(f"{tag}_{n}", shape, dt))
        sem = Semaphores(nc, ctx, tag)
        gated_buffers(g, sb)
        raw = sb("raw", [P, 2, REC])
        w = [sb(f"w{q}", [P, 2, REC_W1 + REC_W2], F32R) for q in range(2)]
        bias = sb("bias", [P, 2, 3, IC])
        b1v = lambda s: raw[:, s, REC_W1 + REC_W2:REC].rearrange("p (c h) -> p h c", c=IC)
        gate_w = sb("gate_w", [P, KC, E])
        gate_r = [sb(f"gate_r{q}", [P, KC, E], F32R) for q in range(2)]
        gate_b = sb("gate_b", [P, E])
        b2 = sb("b2", [E, D])
        iota = sb("iota", [P, E])
        later = sb("later", [P, HID])
        logits = sb("logits", [P, TILES, E])
        top = sb("top", [P, TILES, 8])
        top_at = sb("top_at", [P, TILES, 8], U32)
        top_atf = sb("top_atf", [P, TILES, 2])
        margin = sb("margin", [P, TILES])
        route = sb("route", [P, 2, TILES])
        pick = sb("pick", [P, 2, TILES, E])
        we = sb("we", [P, TILES, E])
        we_t = g.xn[0:E, :, :, :].rearrange("e q i d -> e (q i d)")

        consts, small_here = sem("consts"), sem("small_here")
        x_here = [sem(f"x_here{b}") for b in range(BATCH)]
        rec_here = [sem(f"rec_here{s}") for s in range(2)]
        pool_const, split_done = sem("pool_const"), sem("split_done")
        gate_split, logits_ready, logits_added = sem("gate_split"), sem("logits_ready"), sem("logits_added")
        routed, margin_done, route_done, we_done = sem("routed"), sem("margin_done"), sem("route_done"), sem("we_done")
        we_turned, we_t_done, b2_ready, b2_added = sem("we_turned"), sem("we_t_done"), sem("b2_ready"), sem("b2_added")

        norm = Norm(nc, sem, g, "norm", 2)

        def weights(n0):
            s, c = (n0 // 8) % 2, n0 % IC
            col = lambda part: (lambda k, half: w[part][:, s, k * 512 + c * 256 + half * P:
                                                        k * 512 + c * 256 + half * P + P])
            o = REC_W1 + c * D
            return Weights(hi=col(0), lo=col(1), out_hi=w[0][:, s, o:o + D],
                                   out_lo=w[1][:, s, o:o + D])

        def rhs(n0, it, k, low):
            b = (n0 % 8) // IC
            return g.xt[low][:, k, b * SEQ:(b + 1) * SEQ]

        def before_first(pe, n0, it):
            if n0 % 8 == 0:
                pe.wait_ge(split_done, 3 * (n0 // 8 + 2 * it + 1))
            if n0 < 8 and n0 % IC == 0:
                pe.wait_ge(norm.lo_done, n0 // IC + 1)

        def biases(n0):
            s, c = (n0 // 8) % 2, n0 % IC
            return Biases(sig=bias[:, s, 0, c:c + 1], scale=1.702, gate=bias[:, s, 1, c:c + 1],
                                   lin=bias[:, s, 2, c:c + 1])

        def scale(m0, it, i):
            return we[:, (m0 % BATCH) * BT + i, bass.ds(m0 // BATCH + 2 * it, 1)]

        def xr(m0, it, i):
            return g.x[:, (m0 % BATCH) * BT + i, :]

        if which == 0:
            jobs = [(g.wqkv, k, "wqkv", 3 * D) for k in range(KC)] + [(g.wout, k, "wout", D) for k in range(KC)]
        else:
            jobs = [(t, k, name, n) for t, name, n in ((g.lqkv, "lqkv", 2 * D), (g.lout, "lout", D),
                                                       (g.w1, "w1", HID), (g.w3, "w3", HID)) for k in range(KC)]
        later_here, later_split = sem("later_here"), sem("later_split")

        def load_later(sp):
            for j, (_, k, name, n) in enumerate(jobs):
                if j:
                    sp.wait_ge(later_split, 2 * j)
                sp.dma_start(later[:, 0:n], ins[name][:, k, :]).then_inc(later_here, 16)

        def split_later(pool):
            for j, (t, k, _, n) in enumerate(jobs):
                pool.wait_ge(later_here, 16 * (j + 1))
                split_weights(nc, pool, later_split, 2 * j, t[0][:, k, :], t[1][:, k, :], later[:, 0:n])

        units = Gated(nc, sem, g, "unit", E * BATCH * IC, 16, IC, 2, before_first, weights, rhs, biases, scale, xr)
        block = ctx.enter_context(nc.Block())
        x_block = x_of(g)

        @block.sync
        def _(sp):
            if which == 0:
                for b in range(BATCH):
                    sp.dma_start(g.x[:, b * BT:(b + 1) * BT, :], x_dram[:, b * BT:(b + 1) * BT, :]) \
                        .then_inc(x_here[b], 16)
                    if b == 0:
                        sp.dma_start(g.ident[:, :], ins["ident"]).then_inc(consts, 16)
            sp.dma_start(gate_w[:, :, :], ins["gate_w"]).then_inc(small_here, 16)
            sp.dma_start(gate_b[:, :], ins["gate_b"].rearrange("(a e) -> a e", a=1).partition_broadcast(P)) \
                .then_inc(small_here, 16)
            sp.dma_start(b2[:, :], ins["b2"]).then_inc(small_here, 16)
            sp.dma_start(iota[:, :], ins["iota"]).then_inc(small_here, 16)
            for e in range(E):
                if e == 2:
                    load_later(sp)
                if e >= 2:
                    sp.wait_ge(split_done, 3 * (e - 1))
                sp.dma_start(raw[:, e % 2, :], ins["moe"][e]).then_inc(rec_here[e % 2], 16)

        @block.gpsimd
        def _(pool):
            if which == 0:
                nc.gpsimd.memset(g.neg_half[:, :], -0.5).then_inc(pool_const, 1)
                nc.gpsimd.memset(g.eps[:, :], EPS).then_inc(pool_const, 1)
                pool.wait_ge(pool_const, 2)

            def split(e, s):
                pool.wait_ge(rec_here[s], 16 * (e // 2 + 1))
                if e >= 2:
                    pool.wait_ge(units.y_free, 4 + 8 * (e - 1))
                split_weights(nc, pool, split_done, 3 * e, w[0][:, s, :], w[1][:, s, :],
                              raw[:, s, 0:REC_W1 + REC_W2])
                nc.gpsimd.tensor_scalar(bias[:, s, 0, :], b1v(s)[:, 0, :], 1.702, None, ALU.mult)
                nc.gpsimd.tensor_scalar(bias[:, s, 1, :], b1v(s)[:, 0, :], 0.0, None, ALU.add)
                nc.gpsimd.tensor_scalar(bias[:, s, 2, :], b1v(s)[:, 1, :], 1.0, None, ALU.add) \
                    .then_inc(split_done, 1)
            norm.rstd(pool, 0)
            split(0, 0)
            for b in range(1, BATCH):
                norm.rstd(pool, b)
            split(1, 1)
            split_later(pool)
            for e in range(2, E):
                split(e, e % 2)

        @block.tensor
        def _(pe):
            if which == 0:
                pe.wait_ge(consts, 16)
            norm_pe(norm, pe)
            pe.wait_ge(norm.lo_done, BATCH)
            pe.wait_ge(gate_split, 2)
            for t in range(TILES):
                steps = [(a, b, k) for k in range(KC) for a, b in ((0, 0), (0, 1), (1, 0))]
                for q, (a, b, k) in enumerate(steps):
                    last = nc.tensor.matmul(g.ps[:, 4, t * E:(t + 1) * E], g.xt[a][:, k, t * P:(t + 1) * P],
                                            gate_r[b][:, k, :], start=(q == 0), stop=(q == len(steps) - 1))
            last.then_inc(logits_ready, 1)
            pe.wait_ge(we_done, 1)
            for t in range(TILES):
                last = nc.tensor.transpose(g.ps[0:E, 4 + t // 4, (t % 4) * P:(t % 4 + 1) * P],
                                           we[:, t, :], g.ident[:, :])
            last.then_inc(we_turned, 1)
            pe.wait_ge(we_t_done, 1)
            for half in range(2):
                if half:
                    pe.wait_ge(b2_added, 1)
                for t in range(8):
                    last = nc.tensor.matmul(g.ps[:, 4 + t // 2, (t % 2) * D:(t % 2 + 1) * D],
                                            we_t[:, (8 * half + t) * P:(8 * half + t + 1) * P], b2[:, :],
                                            start=True, stop=True)
                last.then_inc(b2_ready, 1)
            pe.wait_ge(b2_added, 2)
            units.run_pe(pe)

        @block.scalar
        def _(act):
            norm_act(norm, act, g.xt)
            act.wait_ge(margin_done, 1)
            nc.scalar.activation(route[:, 0, :], margin[:, :], ACT.Sigmoid, scale=-1.0).then_inc(route_done, 1)
            nc.scalar.activation(route[:, 1, :], margin[:, :], ACT.Sigmoid).then_inc(route_done, 1)
            act.wait_ge(we_turned, 1)
            nc.scalar.activation(we_t[:, :], g.ps[0:E, 4:8, :].rearrange("e b n -> e (b n)"), ACT.Copy) \
                .then_inc(we_t_done, 1)
            units.run_act(act)

        @block.vector
        def _(dve):
            norm_dve(norm, dve, g.xt, x_block, x_here if which == 0 else None)
            dve.wait_ge(small_here, 64)
            nc.vector.tensor_copy(gate_r[0][:, :, :], gate_w[:, :, :]).then_inc(gate_split, 1)
            dve.wait_ge(gate_split, 1)
            nc.vector.tensor_tensor(gate_r[1][:, :, :], gate_w[:, :, :], f32(gate_r[0][:, :, :]), ALU.subtract) \
                .then_inc(gate_split, 1)
            dve.wait_ge(logits_ready, 1)
            nc.vector.tensor_tensor(logits[:, :, :], g.ps[:, 4, 0:TILES * E].rearrange("p (t e) -> p t e", e=E),
                                    gate_b[:, :].unsqueeze(1).to_broadcast([P, TILES, E]), ALU.add) \
                .then_inc(logits_added, 1)
            dve.wait_ge(logits_added, 1)
            for t in range(TILES):
                last = nc.vector.max(top[:, t, :], logits[:, t, :])
            last.then_inc(routed, 1)
            dve.wait_ge(routed, 1)
            nc.vector.tensor_tensor(margin[:, :], top[:, :, 1], top[:, :, 0], ALU.subtract).then_inc(margin_done, 1)
            for t in range(TILES):
                last = nc.vector.max_index(top_at[:, t, :], top[:, t, :], logits[:, t, :])
            last.then_inc(routed, 1)
            dve.wait_ge(routed, 2)
            nc.vector.tensor_copy(top_atf[:, :, :], top_at[:, :, 0:2]).then_inc(routed, 1)
            dve.wait_ge(routed, 3)
            for r in range(2):
                last = nc.vector.tensor_tensor(pick[:, r, :, :], top_atf[:, :, r:r + 1].to_broadcast([P, TILES, E]),
                                               iota[:, :].unsqueeze(1).to_broadcast([P, TILES, E]), ALU.is_equal)
            last.then_inc(routed, 1)
            dve.wait_ge(routed, 4)
            dve.wait_ge(route_done, 2)
            for r in range(2):
                last = nc.vector.tensor_tensor(pick[:, r, :, :], pick[:, r, :, :],
                                               route[:, r, :].unsqueeze(2).to_broadcast([P, TILES, E]), ALU.mult)
            last.then_inc(routed, 1)
            dve.wait_ge(routed, 5)
            nc.vector.tensor_tensor(we[:, :, :], pick[:, 0, :, :], pick[:, 1, :, :], ALU.add).then_inc(routed, 1)
            dve.wait_ge(routed, 6)
            nc.vector.tensor_scalar(we[:, :, :], we[:, :, :], 0.5, None, ALU.mult).then_inc(we_done, 1)
            for half in range(2):
                dve.wait_ge(b2_ready, half + 1)
                xs = g.x[:, 8 * half:8 * half + 8, :].rearrange("p t d -> p (t d)")
                nc.vector.tensor_tensor(xs, xs, g.ps[:, 4:8, :].rearrange("p b n -> p (b n)"), ALU.add) \
                    .then_inc(b2_added, 1)
            dve.wait_ge(b2_added, 2)
            units.run_dve(dve)


def attention_stage(nc, g, ins):
    with ExitStack() as ctx:
        sb = lambda n, shape, dt=F32: ctx.enter_context(nc.sbuf_tensor(f"att_{n}", shape, dt))
        sem = Semaphores(nc, ctx, "att")
        g.xn = sb("xn", [P, 1, BT, D])
        xt = [sb(f"xt{q}", [P, KC, SEQ], F32R) for q in range(2)]
        bqkv = sb("bqkv", [P, 3 * D])
        bout = sb("bout", [P, D])
        rope_c = sb("rope_c", [P, BT, HD])
        rope_s = sb("rope_s", [P, BT, HD])
        mask = sb("mask", [P, SEQ])
        qk = sb("qk", [P, 2, 2 * D])
        v = sb("v", [P, BT, D])
        part_a = sb("part_a", [P, 2, 2 * D])
        part_b = sb("part_b", [P, 2, 2 * D])
        rot = sb("rot", [P, 2, 2 * D])
        stack = [sb(f"stack{q}", [P, 2, H, 2, 2, HD], F32R) for q in range(2)]
        turned_t = [sb(f"turned{q}", [P, H // 2, SEQ], F32R) for q in range(2)]
        SC, PR, PT = 3, 6, 4
        scores = sb("scores", [P, SC, SEQ])
        probs = sb("probs", [P, PR, SEQ])
        probs_t = sb("probs_t", [P, PT, SEQ])
        neg_max = sb("neg_max", [P, BT, H])
        row_sum = sb("row_sum", [P, BT, H])
        inv_sum = sb("inv_sum", [P, BT, H])
        context = g.xn[:, 0, :, :]

        consts = sem("consts")
        proj_ps, qkv_added, rope_a_done, rope_b_done, rot_done = (
            sem("proj_ps"), sem("qkv_added"), sem("rope_a_done"), sem("rope_b_done"), sem("rot_done"))
        hi_done, q_lo_done, k_lo_done = sem("hi_done"), sem("q_lo_done"), sem("k_lo_done")
        stack_turned, qt_done, kt_done = sem("stack_turned"), sem("qt_done"), sem("kt_done")
        scores_ps, scores_done, probs_done = sem("scores_ps"), sem("scores_done"), sem("probs_done")
        probs_turned, pv_done = sem("probs_turned"), sem("pv_done")
        pt_done = [sem("pt_done_act"), sem("pt_done_dve")]
        inv_done, context_done, context_turned = sem("inv_done"), sem("context_done"), sem("context_turned")
        context_hi, context_lo, out_ps, x_biased, x_added = (
            sem("context_hi"), sem("context_lo"), sem("out_ps"), sem("x_biased"), sem("x_added"))
        x_stored, x_turned = sem("x_stored"), sem("x_turned")
        norm = Norm(nc, sem, g, "norm", 1)

        xf = g.x[:, :, :].rearrange("p t d -> p (t d)")
        x_tile = lambda it: (lambda i: xf[:, bass.ds(it * (BT * D) + i * D, D)])
        x_row = lambda it: xf[:, bass.ds(it * (BT * D), BT * D)]
        items = [(h, i) for h in range(H) for i in range(BT)]
        N = len(items)
        S_BANKS, PT_BANKS, CTX_BANK = (0, 1, 2), (3, 4, 7), 5
        NS, NPT = len(S_BANKS), len(PT_BANKS)
        TURN, COPY, WEIGH = 3, 4, 5
        copies = lambda w: 0 if items[w][1] < 2 else 1
        copied = lambda w: sum(copies(u) == copies(w) for u in range(w + 1))
        per_trip = [sum(copies(u) == q for u in range(N)) for q in range(2)]

        def copy_probs(eng, it, w):
            h, i = items[w]
            eng.wait_ge(probs_turned, N * it + w + 1)
            if w >= PT:
                eng.wait_ge(pv_done, N * it + w - PT + 1)
            src, dst = g.ps[:, PT_BANKS[w % NPT], 0:(i + 1) * P], probs_t[:, w % PT, 0:(i + 1) * P]
            if copies(w) == 0:
                nc.scalar.activation(dst, src, ACT.Copy).then_inc(pt_done[0], 1)
            else:
                nc.vector.tensor_copy(dst, src).then_inc(pt_done[1], 1)

        block = ctx.enter_context(nc.Block())

        @block.sync
        def _(sp):
            row = lambda ap: ap.rearrange("(a n) -> a n", a=1).partition_broadcast(P)
            for dst, src in ((bqkv[:, :], row(ins["bqkv"])), (rope_c[:, :, :], ins["rope_c"]),
                             (rope_s[:, :, :], ins["rope_s"]), (mask[:, :], ins["mask"]),
                             (bout[:, :], row(ins["bout"]))):
                sp.dma_start(dst, src).then_inc(consts, 16)
            for b in range(BATCH):
                sp.wait_ge(x_added, b + 1)
                sp.dma_start(by_tiles(g.turned_dram[0], b), g.x[:, b * BT:(b + 1) * BT, :]).then_inc(x_stored, 16)
            sp.wait_ge(x_stored, 16 * BATCH)
            for b in range(BATCH):
                at = slice(b * BATCH_P, (b + 1) * BATCH_P)
                sp.dma_start(g.x[at, :, :], by_sixteens(g.turned_dram[0])[at]).then_inc(x_turned, 16)
            sp.wait_ge(x_turned, 16 * BATCH)

        CONSTS = 16 * 5

        @block.gpsimd
        def _(pool):
            pool.wait_ge(consts, CONSTS)
            for it in range(BATCH):
                norm.rstd(pool, it)
                pool.wait_ge(norm.xn_done, it + 1)
                x_tiles = x_row(it).rearrange("p (t d) -> p t d", d=D)
                nc.gpsimd.tensor_tensor(x_tiles, x_tiles,
                                        bout[:, :].unsqueeze(1).to_broadcast([P, BT, D]), ALU.add).then_inc(x_biased, 1)

                def swapped(i):
                    pool.wait_ge(qkv_added, 4 * it + i + 1)
                    src = qk[:, i % 2, :].rearrange("p (h s e) -> p h s e", s=2, e=HALF)
                    dst = part_b[:, i % 2, :].rearrange("p (h s e) -> p h s e", s=2, e=HALF)
                    if i >= 2:
                        pool.wait_ge(rot_done, 4 * it + i - 1)
                    for s in range(2):
                        last = nc.gpsimd.tensor_tensor(
                            dst[:, :, s, :], src[:, :, 1 - s, :],
                            rope_s[:, i, s * HALF:(s + 1) * HALF].unsqueeze(1).to_broadcast([P, 2 * H, HALF]),
                            ALU.mult)
                    last.then_inc(rope_b_done, 1)

                def q_low(i):
                    pool.wait_ge(hi_done, 4 * it + i + 1)
                    r = rot[:, i % 2, 0:D].rearrange("p (h d) -> p h d", d=HD)
                    for c in range(2):
                        last = nc.gpsimd.tensor_tensor(stack[0][:, i % 2, :, 1, c, :], r,
                                                       f32(stack[0][:, i % 2, :, 0, 0, :]), ALU.subtract)
                    last.then_inc(q_lo_done, 1)

                for i in range(BT + 1):
                    if i < BT:
                        swapped(i)
                    if i:
                        q_low(i - 1)

        @block.tensor
        def _(pe):
            for it in range(BATCH):
                norm.turn(pe, it, 0)
                pe.wait_ge(norm.lo_done, it + 1)
                for i in range(BT):
                    if i >= 2:
                        pe.wait_ge(qkv_added, 4 * it + i - 1)
                    for out, cols in ((g.ps[:, i % 2, :], slice(0, 2 * D)),
                                      (g.ps[:, 2 + i % 2, 0:D], slice(2 * D, 3 * D))):
                        steps = [(k, a, b) for k in range(KC) for a, b in ((0, 0), (0, 1), (1, 0))]
                        for q, (k, a, b) in enumerate(steps):
                            last = nc.tensor.matmul(out, xt[a][:, k, i * P:(i + 1) * P], g.wqkv[b][:, k, cols],
                                                    start=(q == 0), stop=(q == len(steps) - 1))
                    last.then_inc(proj_ps, 1)
                for i in range(BT):
                    pe.wait_ge(q_lo_done, 4 * it + i + 1)
                    pe.wait_ge(k_lo_done, 4 * it + i + 1)
                    pe.wait_ge(qt_done, 4 * it + i)
                    pe.wait_ge(kt_done, 4 * it + i)
                    for s in range(2):
                        flat = f32(stack[s][:, i % 2, :, :, :, :]).rearrange("p h a b d -> p (h a b d)")
                        for hp in range(H // 2):
                            last = nc.tensor.transpose(g.ps[:, 4 + 2 * s + hp // 4, (hp % 4) * P:(hp % 4 + 1) * P],
                                                       flat[:, hp * P:(hp + 1) * P], g.ident[:, :])
                    last.then_inc(stack_turned, 1)
                pe.wait_ge(qt_done, 4 * it + 4)
                pe.wait_ge(kt_done, 4 * it + 4)

                def score(w):
                    h, i = items[w]
                    r = 64 * (h % 2)
                    if w >= NS:
                        pe.wait_ge(scores_done, N * it + w - NS + 1)
                    nc.tensor.matmul(g.ps[:, S_BANKS[w % NS], 0:(i + 1) * P],
                                     turned_t[0][r:r + 64, h // 2, i * P:(i + 1) * P],
                                     turned_t[1][r:r + 64, h // 2, 0:(i + 1) * P],
                                     start=True, stop=True).then_inc(scores_ps, 1)

                def turn(w):
                    h, i = items[w]
                    pe.wait_ge(probs_done, N * it + w + 1)
                    if w >= NPT:
                        pe.wait_ge(pt_done[copies(w - NPT)], per_trip[copies(w - NPT)] * it + copied(w - NPT))
                    for j in range(i + 1):
                        last = nc.tensor.transpose(g.ps[:, PT_BANKS[w % NPT], j * P:(j + 1) * P],
                                                   probs[:, w % PR, j * P:(j + 1) * P], g.ident[:, :])
                    last.then_inc(probs_turned, 1)

                def weigh(w):
                    h, i = items[w]
                    pe.wait_ge(pt_done[copies(w)], per_trip[copies(w)] * it + copied(w))
                    at = (i % 2) * D + h * HD
                    for j in range(i + 1):
                        last = nc.tensor.matmul(g.ps[:, CTX_BANK + i // 2, at:at + HD],
                                                probs_t[:, w % PT, j * P:(j + 1) * P],
                                                v[:, j, h * HD:(h + 1) * HD], start=(j == 0), stop=(j == i))
                    last.then_inc(pv_done, 1)

                for w in range(N + WEIGH):
                    if w < N:
                        score(w)
                    if TURN <= w < N + TURN:
                        turn(w - TURN)
                    if w >= WEIGH:
                        weigh(w - WEIGH)
                pe.wait_ge(context_done, it + 1)
                for k in range(KC):
                    for i in range(BT):
                        last = nc.tensor.transpose(g.ps[:, k, i * P:(i + 1) * P],
                                                   context[:, i, k * P:(k + 1) * P], g.ident[:, :])
                last.then_inc(context_turned, 1)
                pe.wait_ge(context_lo, it + 1)
                project_out(nc, g, xt, g.wout).then_inc(out_ps, 1)

        @block.scalar
        def _(act):
            for it in range(BATCH):
                norm.high(act, it, 0, xt[0][:, :, :])

                def high(i):
                    act.wait_ge(rot_done, 4 * it + i + 1)
                    if i >= 2:
                        act.wait_ge(stack_turned, 4 * it + i - 1)
                    r = rot[:, i % 2, :].rearrange("p (s h d) -> p s h d", s=2, d=HD)
                    for c in range(2):
                        nc.scalar.activation(stack[0][:, i % 2, :, 0, c, :], r[:, 0, :, :], ACT.Copy)
                    for a in range(2):
                        last = nc.scalar.activation(stack[1][:, i % 2, :, a, 0, :], r[:, 1, :, :], ACT.Copy)
                    last.then_inc(hi_done, 1)

                def q_out(i):
                    act.wait_ge(stack_turned, 4 * it + i + 1)
                    nc.scalar.activation(turned_t[0][:, :, i * P:(i + 1) * P],
                                         g.ps[:, 4:6, :].rearrange("p b (h t) -> p (b h) t", t=P), ACT.Copy) \
                        .then_inc(qt_done, 1)
                for i in range(BT + 1):
                    if i < BT:
                        high(i)
                    if i:
                        q_out(i - 1)

                def exponentials(w):
                    h, i = items[w]
                    act.wait_ge(scores_done, N * it + w + 1)
                    if w >= PR:
                        act.wait_ge(probs_turned, N * it + w - PR + 1)
                    nc.scalar.activation(probs[:, w % PR, 0:(i + 1) * P], scores[:, w % SC, 0:(i + 1) * P], ACT.Exp,
                                         bias=neg_max[:, i, h:h + 1], scale=-1.0,
                                         accum_out=row_sum[:, i, h:h + 1]).then_inc(probs_done, 1)
                for w in range(N + COPY):
                    if w < N:
                        exponentials(w)
                    if w >= COPY and copies(w - COPY) == 0:
                        copy_probs(act, it, w - COPY)
                act.wait_ge(context_turned, it + 1)
                nc.scalar.activation(xt[0][:, :, :], g.ps[:, 0:KC, :], ACT.Copy).then_inc(context_hi, 1)

        @block.vector
        def _(dve):
            dve.wait_ge(consts, CONSTS)
            for it in range(BATCH):
                dve.wait_ge(x_added, it)
                norm.stats(dve, it, x_tile(it))
                norm.normalise(dve, it, x_tile(it))
                norm.low(dve, it, 0, xt[0][:, :, :], xt[1][:, :, :])

                def rotate(i):
                    dve.wait_ge(proj_ps, 4 * it + i + 1)
                    nc.vector.tensor_tensor(qk[:, i % 2, :], g.ps[:, i % 2, :], bqkv[:, 0:2 * D], ALU.add)
                    nc.vector.tensor_tensor(v[:, i, :], g.ps[:, 2 + i % 2, 0:D], bqkv[:, 2 * D:3 * D], ALU.add) \
                        .then_inc(qkv_added, 1)
                    dve.wait_ge(qkv_added, 4 * it + i + 1)
                    heads = lambda t: t[:, i % 2, :].rearrange("p (h d) -> p h d", d=HD)
                    nc.vector.tensor_tensor(heads(part_a), heads(qk),
                                            rope_c[:, i, :].unsqueeze(1).to_broadcast([P, 2 * H, HD]), ALU.mult) \
                        .then_inc(rope_a_done, 1)
                    if i >= 2:
                        dve.wait_ge(q_lo_done, 4 * it + i - 1)
                    dve.wait_ge(rope_a_done, 4 * it + i + 1)
                    dve.wait_ge(rope_b_done, 4 * it + i + 1)
                    nc.vector.tensor_tensor(rot[:, i % 2, :], part_a[:, i % 2, :], part_b[:, i % 2, :], ALU.add) \
                        .then_inc(rot_done, 1)

                def k_low(i):
                    dve.wait_ge(hi_done, 4 * it + i + 1)
                    r = rot[:, i % 2, D:2 * D].rearrange("p (h d) -> p h d", d=HD)
                    for a in range(2):
                        last = nc.vector.tensor_tensor(stack[1][:, i % 2, :, a, 1, :], r,
                                                       f32(stack[1][:, i % 2, :, 0, 0, :]), ALU.subtract)
                    last.then_inc(k_lo_done, 1)

                def k_out(i):
                    dve.wait_ge(stack_turned, 4 * it + i + 1)
                    nc.vector.tensor_copy(turned_t[1][:, :, i * P:(i + 1) * P],
                                          g.ps[:, 6:8, :].rearrange("p b (h t) -> p (b h) t", t=P)) \
                        .then_inc(kt_done, 1)
                for i in range(BT + 2):
                    if i < BT:
                        rotate(i)
                    if 1 <= i <= BT:
                        k_low(i - 1)
                    if i >= 2:
                        k_out(i - 2)

                def masked(w):
                    h, i = items[w]
                    dve.wait_ge(scores_ps, N * it + w + 1)
                    if w >= SC:
                        dve.wait_ge(probs_done, N * it + w - SC + 1)
                    nc.vector.tensor_tensor_reduce(scores[:, w % SC, 0:(i + 1) * P],
                                                   g.ps[:, S_BANKS[w % NS], 0:(i + 1) * P],
                                                   mask[:, SEQ - (i + 1) * P:SEQ], -(HD ** -0.5), 3.0e38,
                                                   ALU.add, ALU.min, neg_max[:, i, h:h + 1]).then_inc(scores_done, 1)
                for w in range(N + COPY):
                    if w < N:
                        masked(w)
                    if w >= COPY and copies(w - COPY) == 1:
                        copy_probs(dve, it, w - COPY)
                dve.wait_ge(pv_done, N * it + N)
                nc.vector.reciprocal(inv_sum[:, :, :], row_sum[:, :, :]).then_inc(inv_done, 1)
                dve.wait_ge(inv_done, it + 1)
                nc.vector.tensor_tensor(
                    context[:, :, :].rearrange("p t (h d) -> p (t h) d", d=HD),
                    g.ps[:, CTX_BANK:CTX_BANK + 2, :].rearrange("p b (h d) -> p (b h) d", d=HD),
                    inv_sum[:, :, :].rearrange("p t h -> p (t h)").unsqueeze(2).to_broadcast([P, BT * H, HD]),
                    ALU.mult).then_inc(context_done, 1)
                dve.wait_ge(context_hi, it + 1)
                nc.vector.tensor_tensor(xt[1][:, :, :], g.ps[:, 0:KC, :], f32(xt[0][:, :, :]), ALU.subtract) \
                    .then_inc(context_lo, 1)
                dve.wait_ge(x_biased, it + 1)
                dve.wait_ge(out_ps, it + 1)
                nc.vector.tensor_tensor(x_row(it), x_row(it), g.ps[:, 2:4, :].rearrange("p b n -> p (b n)"), ALU.add) \
                    .then_inc(x_added, 1)


def project_out(nc, g, xt, w):
    for i in range(BT):
        steps = [(k, a, b) for k in range(KC) for a, b in ((0, 0), (0, 1), (1, 0))]
        for q, (k, a, b) in enumerate(steps):
            last = nc.tensor.matmul(g.ps[:, 2 + i // 2, (i % 2) * D:(i % 2 + 1) * D],
                                    xt[a][:, k, i * P:(i + 1) * P], w[b][:, k, :],
                                    start=(q == 0), stop=(q == len(steps) - 1))
    return last


def hadamard_stage(nc, g, ins, which):
    with ExitStack() as ctx:
        tag = f"had{which}"
        sb = lambda n, shape, dt=F32: ctx.enter_context(nc.sbuf_tensor(f"{tag}_{n}", shape, dt))
        sem = Semaphores(nc, ctx, tag)
        gated_buffers(g, sb)
        norm = Norm(nc, sem, g, "norm", 2)
        if which == 0:
            raw = sb("w2raw", [P, HC, D])
            part = [sb(f"w2part{q}", [P, HC, D], F32R) for q in range(2)]
            had = sb("had", [P, 2, P])
            had_r = sb("had_r", [P, 2, P], F32R)
        here, w2_split, had_ready, mixed, w2_hi, w2_lo = (
            sem("here"), sem("w2_split"), sem("had_ready"), sem("mixed"), sem("w2_hi"), sem("w2_lo"))

        def weights(n0):
            hc = n0 % HC
            col = lambda q: (lambda k, half: (g.w1, g.w3)[half][q][:, k, hc * P:(hc + 1) * P])
            return Weights(hi=col(0), lo=col(1), out_hi=g.w2[0][:, hc, :], out_lo=g.w2[1][:, hc, :])

        def rhs(n0, it, k, low):
            return g.xt[low][:, k, bass.ds((n0 // HC + it) * SEQ, SEQ)]

        def before_first(pe, n0, it):
            if n0 % HC == 0:
                pe.wait_ge(norm.lo_done, n0 // HC + it + 1)

        def xr(m0, it, i):
            return g.x[:, :, :].rearrange("p t d -> p (t d)")[:, bass.ds((m0 + it) * (BT * D) + i * D, D)]

        units = Gated(nc, sem, g, "unit", HC * BATCH, HC, HC, 1, before_first, weights, rhs,
                      lambda n0: Biases(sig=0.0, scale=1.0, gate=0.0, lin=0.0),
                      lambda m0, it, i: 0.5, xr)
        block = ctx.enter_context(nc.Block())
        x_block = x_of(g)

        if which == 0:
            @block.sync
            def _(sp):
                sp.dma_start(raw[:, :, :], ins["w2"]).then_inc(here, 16)
                sp.dma_start(had[:, :, :], ins["had"]).then_inc(here, 16)

        @block.gpsimd
        def _(pool):
            if which == 0:
                pool.wait_ge(here, 32)
                nc.gpsimd.tensor_copy(had_r[:, :, :], had[:, :, :]).then_inc(had_ready, 1)
                split_weights(nc, pool, w2_split, 0, part[0][:, :, :], part[1][:, :, :], raw[:, :, :])
            for b in range(BATCH):
                norm.rstd(pool, b)

        @block.tensor
        def _(pe):
            norm_pe(norm, pe)
            if which == 0:
                pe.wait_ge(norm.lo_done, BATCH)
                pe.wait_ge(had_ready, 1)
                pe.wait_ge(w2_split, 2)
                for o in range(HC):
                    for q in range(2):
                        for j in range(HC):
                            odd = bin(o & j).count("1") % 2
                            last = nc.tensor.matmul(g.ps[:, 4 + o // 2, (o % 2) * D:(o % 2 + 1) * D],
                                                    had_r[:, odd, :], part[q][:, j, :],
                                                    start=(q == 0 and j == 0), stop=(q == 1 and j == HC - 1))
                last.then_inc(mixed, 1)
                pe.wait_ge(w2_lo, 1)
            units.run_pe(pe)

        @block.scalar
        def _(act):
            norm_act(norm, act, g.xt)
            if which == 0:
                act.wait_ge(mixed, 1)
                nc.scalar.activation(g.w2[0][:, :, :].rearrange("p c d -> p (c d)"),
                                     g.ps[:, 4:8, :].rearrange("p b n -> p (b n)"), ACT.Copy,
                                     scale=HID ** -0.5).then_inc(w2_hi, 1)
            units.run_act(act)

        @block.vector
        def _(dve):
            norm_dve(norm, dve, g.xt, x_block)
            if which == 0:
                dve.wait_ge(w2_hi, 1)
                nc.vector.scalar_tensor_tensor(
                    out=g.w2[1][:, :, :].rearrange("p c d -> p (c d)"),
                    in0=g.ps[:, 4:8, :].rearrange("p b n -> p (b n)"), scalar=HID ** -0.5,
                    in1=f32(g.w2[0][:, :, :]).rearrange("p c d -> p (c d)"),
                    op0=ALU.mult, op1=ALU.subtract).then_inc(w2_lo, 1)
            units.run_dve(dve)


def features_stage(nc, g, ins):
    QKH = H + HKV
    TWO_PI = 2.0 * np.pi
    ROUND = 1.5 * 2.0 ** 23
    with ExitStack() as ctx:
        sb = lambda n, shape, dt=F32: ctx.enter_context(nc.sbuf_tensor(f"fea_{n}", shape, dt))
        sem = Semaphores(nc, ctx, "fea")
        g.xn = sb("xn", [P, 1, BT, D])
        xt = [sb(f"xt{q}", [P, KC, SEQ], F32R) for q in range(2)]
        bias = sb("bias", [P, 2 * D])
        bout = sb("bout", [P, D])
        rope_c = sb("rope_c", [P, TILES, HD])
        rope_s = sb("rope_s", [P, TILES, HD])
        rand_blocks = sb("rand_blocks", [P, (P // HD) * HALF])
        qkv = sb("qkv", [P, BT, 2 * D])
        part_a = sb("part_a", [P, BT, QKH * HD])
        part_b = sb("part_b", [P, BT, QKH * HD])
        rot = sb("rot", [P, BT, QKH * HD])
        square_sum = sb("square_sum", [P, BT * QKH])
        inv_norm = sb("inv_norm", [P, BT * QKH])
        rot_t = sb("rot_t", [P, 3, SEQ])
        turns = sb("turns", [P, BT * QKH, 2, HALF])
        features = sb("features", [P, BT, QKH, HD])
        qk_prod = sb("qk_prod", [P, 2, H, HKV, HD])
        wv_prod = sb("wv_prod", [P, H, HD, HKV])
        weight = sb("weight", [P, 2, H * HKV])
        v_scaled = sb("v_scaled", [P, BT, HKV * HD])
        context = sb("context", [P, H, TILES, HD])

        consts, zeroed = sem("consts"), sem("zeroed")
        s = Shared()
        s.proj_ps, s.added, s.v_done = sem("proj_ps"), sem("added"), sem("v_done")
        s.rope_a_done, s.rope_b_done, s.rot_done = sem("rope_a_done"), sem("rope_b_done"), sem("rot_done")
        s.squared, s.summed, s.clamped = sem("squared"), sem("summed"), sem("clamped")
        s.inv_done, s.rot_turned, s.rot_out = sem("inv_done"), sem("rot_turned"), sem("rot_out")
        s.angles_ps, s.sin_turns, s.turns_done = sem("angles_ps"), sem("sin_turns"), sem("turns_done")
        s.whole_done, s.rest_done, s.features_done = sem("whole_done"), sem("rest_done"), sem("features_done")
        s.qk_done, s.weight_done, s.wv_done = sem("qk_done"), sem("weight_done"), sem("wv_done")
        s.x_stored, s.x_turned, s.context_done = sem("x_stored"), sem("x_turned"), sem("context_done")
        s.context_turned, s.context_hi, s.context_lo = sem("context_turned"), sem("context_hi"), sem("context_lo")
        s.out_ps, s.x_biased, s.x_added = sem("out_ps"), sem("x_biased"), sem("x_added")
        norm = Norm(nc, sem, g, "norm", 1)
        x_tile = lambda it: (lambda i: g.x[:, it * BT + i, :])
        x_block = lambda it: g.x[:, it * BT:(it + 1) * BT, :]
        heads = lambda t: t.rearrange("p t (h d) -> p t h d", d=HD)
        CONSTS = 16 * (4 + P // HD)

        block = ctx.enter_context(nc.Block())

        @block.sync
        def _(sp):
            row = lambda ap: ap.rearrange("(a n) -> a n", a=1).partition_broadcast(P)
            for dst, src in ((bias[:, :], row(ins["lbias"])), (rope_c[:, :, :], ins["rope_c16"]),
                             (rope_s[:, :, :], ins["rope_s16"]), (bout[:, :], row(ins["lbout"]))):
                sp.dma_start(dst, src).then_inc(consts, 16)
            sp.dma_start(by_sixteens(g.turned_dram[1]), g.x[:, :, :]).then_inc(s.x_stored, 16)
            sp.wait_ge(zeroed, 1)
            for n in range(P // HD):
                sp.dma_start(rand_blocks[n * HD:(n + 1) * HD, n * HALF:(n + 1) * HALF], ins["rand"]) \
                    .then_inc(consts, 16)
            sp.wait_ge(norm.xn_done, BATCH)
            sp.wait_ge(s.x_stored, 16)
            for b in range(BATCH):
                sp.dma_start(g.x[b * BATCH_P:(b + 1) * BATCH_P, :, :], by_heads(g.turned_dram[1], b)) \
                    .then_inc(s.x_turned, 16)

        @block.gpsimd
        def _(pool):
            nc.gpsimd.memset(rand_blocks[:, :], 0.0).then_inc(zeroed, 1)
            pool.wait_ge(consts, CONSTS)
            for it in range(BATCH):
                norm.rstd(pool, it)
                pool.wait_ge(s.added, 4 * it + 4)
                src = qkv[:, :, 0:QKH * HD].rearrange("p t (h s e) -> p t h s e", s=2, e=HALF)
                dst = part_b[:, :, :].rearrange("p t (h s e) -> p t h s e", s=2, e=HALF)
                for i in range(BT):
                    for q in range(2):
                        last = nc.gpsimd.tensor_tensor(
                            dst[:, i, :, q, :], src[:, i, :, 1 - q, :],
                            rope_s[:, it * BT + i, q * HALF:(q + 1) * HALF].unsqueeze(1).to_broadcast([P, QKH, HALF]),
                            ALU.mult)
                last.then_inc(s.rope_b_done, 1)
                pool.wait_ge(s.clamped, it + 1)
                for q in range(2):
                    at = slice(q * BT * QKH // 2, (q + 1) * BT * QKH // 2)
                    last = nc.gpsimd.tensor_tensor(inv_norm[:, at], square_sum[:, at], g.neg_half[:, 0:BT * QKH // 2],
                                                   ALU.pow)
                last.then_inc(s.inv_done, 1)
                pool.wait_ge(s.features_done, it + 1)
                for i in range(BT):
                    if i >= 2:
                        pool.wait_ge(s.weight_done, 4 * it + i - 1)
                    nc.gpsimd.tensor_tensor(qk_prod[:, i % 2, :, :, :],
                                            features[:, i, 0:H, :].unsqueeze(2).to_broadcast([P, H, HKV, HD]),
                                            features[:, i, H:QKH, :].unsqueeze(1).to_broadcast([P, H, HKV, HD]),
                                            ALU.mult).then_inc(s.qk_done, 1)
            pool.wait_ge(s.x_turned, 16 * BATCH)
            for it in range(BATCH):
                nc.gpsimd.tensor_tensor(x_block(it), x_block(it), bout[:, :].unsqueeze(1).to_broadcast([P, BT, D]),
                                        ALU.add).then_inc(s.x_biased, 1)

        @block.tensor
        def _(pe):
            pe.wait_ge(consts, CONSTS)
            for it in range(BATCH):
                norm.turn(pe, it, 0)
                pe.wait_ge(norm.lo_done, it + 1)
                for i in range(BT):
                    if i >= 2:
                        pe.wait_ge(s.added, 4 * it + i - 1)
                    steps = [(k, a, b) for k in range(KC) for a, b in ((0, 0), (0, 1), (1, 0))]
                    for q, (k, a, b) in enumerate(steps):
                        last = nc.tensor.matmul(g.ps[:, 2 + i % 2, :], xt[a][:, k, i * P:(i + 1) * P],
                                                g.lqkv[b][:, k, :], start=(q == 0), stop=(q == len(steps) - 1))
                    last.then_inc(s.proj_ps, 1)
                pe.wait_ge(s.rot_done, it + 1)
                for k in range(3):
                    for i in range(BT):
                        last = nc.tensor.transpose(g.ps[:, 4 + k, i * P:(i + 1) * P], rot[:, i, k * P:(k + 1) * P],
                                                   g.ident[:, :])
                last.then_inc(s.rot_turned, 1)
                pe.wait_ge(s.rot_out, it + 1)
                for i in range(BT):
                    for k in range(3):
                        at = (i % 2) * QKH * HALF + k * 64
                        last = nc.tensor.matmul(g.ps[:, i // 2, at:at + 64], rot_t[:, k, i * P:(i + 1) * P],
                                                rand_blocks[:, :], start=True, stop=True)
                last.then_inc(s.angles_ps, 1)
            pe.wait_ge(s.context_done, TILES)
            for it in range(BATCH):
                if it:
                    pe.wait_ge(s.x_added, it)
                for k in range(KC):
                    for i in range(BT):
                        row = context[:, it * BT + i, k * (P // HD):(k + 1) * (P // HD), :]
                        last = nc.tensor.transpose(g.ps[:, k, i * P:(i + 1) * P],
                                                   row.rearrange("p a d -> p (a d)"), g.ident[:, :])
                last.then_inc(s.context_turned, 1)
                pe.wait_ge(s.context_lo, it + 1)
                project_out(nc, g, xt, g.lout).then_inc(s.out_ps, 1)

        @block.scalar
        def _(act):
            for it in range(BATCH):
                norm.high(act, it, 0, xt[0][:, :, :])
                act.wait_ge(s.rot_done, it + 1)
                nc.scalar.activation(part_a[:, :, :], rot[:, :, :], ACT.Square).then_inc(s.squared, 1)
                act.wait_ge(s.rot_turned, it + 1)
                nc.scalar.activation(rot_t[:, :, :], g.ps[:, 4:7, :], ACT.Copy).then_inc(s.rot_out, 1)
                act.wait_ge(s.rest_done, it + 1)
                nc.scalar.activation(features[:, :, :, :].rearrange("p t h e -> p (t h e)"),
                                     turns[:, :, :, :].rearrange("p n s e -> p (n s e)"), ACT.Sin,
                                     scale=TWO_PI).then_inc(s.features_done, 1)
            for it in range(BATCH):
                act.wait_ge(s.context_turned, it + 1)
                nc.scalar.activation(xt[0][:, :, :], g.ps[:, 0:KC, :], ACT.Copy).then_inc(s.context_hi, 1)

        @block.vector
        def _(dve):
            dve.wait_ge(consts, CONSTS)
            for it in range(BATCH):
                norm.stats(dve, it, x_tile(it))
                norm.normalise(dve, it, x_tile(it))
                norm.low(dve, it, 0, xt[0][:, :, :], xt[1][:, :, :])
                for i in range(BT):
                    dve.wait_ge(s.proj_ps, 4 * it + i + 1)
                    nc.vector.tensor_tensor(qkv[:, i, :], g.ps[:, 2 + i % 2, :], bias[:, :], ALU.add) \
                        .then_inc(s.added, 1)
                dve.wait_ge(s.added, 4 * it + 4)
                nc.vector.tensor_scalar(v_scaled[:, :, :], qkv[:, :, QKH * HD:2 * D], (H // HKV) / HD, None,
                                        ALU.mult).then_inc(s.v_done, 1)
                nc.vector.tensor_tensor(heads(part_a[:, :, :]), heads(qkv[:, :, 0:QKH * HD]),
                                        rope_c[:, it * BT:(it + 1) * BT, :].unsqueeze(2).to_broadcast([P, BT, QKH, HD]), ALU.mult) \
                    .then_inc(s.rope_a_done, 1)
                dve.wait_ge(s.rope_a_done, it + 1)
                dve.wait_ge(s.rope_b_done, it + 1)
                nc.vector.tensor_tensor(rot[:, :, :], part_a[:, :, :], part_b[:, :, :], ALU.add) \
                    .then_inc(s.rot_done, 1)
                dve.wait_ge(s.squared, it + 1)
                nc.vector.tensor_reduce(square_sum[:, :], part_a[:, :, :].rearrange("p t (h d) -> p (t h) d", d=HD),
                                        AX_X, ALU.add).then_inc(s.summed, 1)
                dve.wait_ge(s.summed, it + 1)
                nc.vector.tensor_scalar(square_sum[:, :], square_sum[:, :], 1e-12, None, ALU.max) \
                    .then_inc(s.clamped, 1)
                dve.wait_ge(s.inv_done, it + 1)
                dve.wait_ge(s.angles_ps, it + 1)
                for c in range(2):
                    last = nc.vector.scalar_tensor_tensor(
                        out=turns[:, c * 2 * QKH:(c + 1) * 2 * QKH, 0, :],
                        in0=g.ps[:, c, 0:2 * QKH * HALF].rearrange("p (n e) -> p n e", e=HALF), scalar=1.0 / TWO_PI,
                        in1=inv_norm[:, c * 2 * QKH:(c + 1) * 2 * QKH].unsqueeze(2).to_broadcast([P, 2 * QKH, HALF]),
                        op0=ALU.mult, op1=ALU.mult)
                last.then_inc(s.sin_turns, 1)
                dve.wait_ge(s.sin_turns, it + 1)
                nc.vector.tensor_scalar(turns[:, :, 1, :], turns[:, :, 0, :], 0.25, None, ALU.add) \
                    .then_inc(s.turns_done, 1)
                dve.wait_ge(s.turns_done, it + 1)
                flat = turns[:, :, :, :].rearrange("p n s e -> p (n s e)")
                whole = part_a[:, :, :].rearrange("p t n -> p (t n)")
                nc.vector.tensor_scalar(whole, flat, ROUND, ROUND, ALU.add, ALU.subtract).then_inc(s.whole_done, 1)
                dve.wait_ge(s.whole_done, it + 1)
                nc.vector.tensor_tensor(flat, flat, whole, ALU.subtract).then_inc(s.rest_done, 1)

                dve.wait_ge(s.v_done, it + 1)

                def weighted(i):
                    dve.wait_ge(s.weight_done, 4 * it + i + 1)
                    dve.wait_ge(s.context_done, 4 * it + i)
                    v_heads = v_scaled[:, i, :].rearrange("p (h d) -> p d h", d=HD)
                    nc.vector.tensor_tensor(
                        wv_prod[:, :, :, :],
                        weight[:, i % 2, :].rearrange("p (h k) -> p h k", k=HKV).unsqueeze(2)
                        .to_broadcast([P, H, HD, HKV]),
                        v_heads.unsqueeze(1).to_broadcast([P, H, HD, HKV]), ALU.mult).then_inc(s.wv_done, 1)
                    dve.wait_ge(s.wv_done, 4 * it + i + 1)
                    nc.vector.tensor_reduce(context[:, :, it * BT + i, :], wv_prod[:, :, :, :],
                                            AX_X, ALU.add).then_inc(s.context_done, 1)
                for i in range(BT):
                    dve.wait_ge(s.qk_done, 4 * it + i + 1)
                    nc.vector.tensor_reduce(weight[:, i % 2, :], qk_prod[:, i % 2, :, :, :]
                                            .rearrange("p h k f -> p (h k) f"), AX_X, ALU.add).then_inc(s.weight_done, 1)
                    if i:
                        weighted(i - 1)
                weighted(BT - 1)
            for it in range(BATCH):
                dve.wait_ge(s.context_hi, it + 1)
                nc.vector.tensor_tensor(xt[1][:, :, :], g.ps[:, 0:KC, :], f32(xt[0][:, :, :]), ALU.subtract) \
                    .then_inc(s.context_lo, 1)
                dve.wait_ge(s.x_biased, it + 1)
                dve.wait_ge(s.out_ps, it + 1)
                nc.vector.tensor_tensor(x_block(it), x_block(it),
                                        g.ps[:, 2:4, :].rearrange("p b (t d) -> p (b t) d", d=D), ALU.add) \
                    .then_inc(s.x_added, 1)


def _laid_out(a):
    c = np.ascontiguousarray
    chunked = lambda w: c(w.reshape(-1, P, w.shape[-1]).transpose(1, 0, 2))
    w1 = a["L0_ffn_w1"].reshape(E, IC, P, 2, KC, P).transpose(0, 5, 4, 1, 3, 2).reshape(E, P, REC_W1)
    w2 = a["L0_ffn_w2"].reshape(E, D, IC, P).transpose(0, 3, 2, 1).reshape(E, P, REC_W2)
    b1 = a["L0_ffn_b1"].reshape(E, IC, P, 2).transpose(0, 2, 1, 3).reshape(E, P, 2 * IC)
    had = np.ones((1, 1), np.float32)
    while had.shape[0] < P:
        had = np.block([[had, had], [had, -had]])
    inv = (1.0 / np.float32(10000.0) ** (np.arange(0, HD, 2, dtype=np.float32) / HD)).astype(np.float32)
    ang = np.outer(np.arange(SEQ, dtype=np.float32), inv)
    cos, sin = np.cos(ang), np.sin(ang)
    tiled = lambda r: c(r.reshape(BT, P, HD).transpose(1, 0, 2).astype(np.float32))
    sixteens = lambda r: c(np.tile(r.reshape(1, BATCH_P, TILES, HD), (BATCH, 1, 1, 1)).reshape(P, TILES, HD)
                           .astype(np.float32))
    mask = np.zeros((P, SEQ), np.float32)
    mask[:, SEQ - P:] = np.triu(np.full((P, P), MASK / HD ** -0.5, np.float32), 1)
    return {
        "x": a["L0_attn_x"], "moe": np.concatenate([w1, w2, b1], axis=2),
        "gate_w": chunked(a["L0_ffn_gate_w"].T), "gate_b": a["L0_ffn_gate_b"], "b2": a["L0_ffn_b2"],
        "wqkv": chunked(a["L0_attn_Wqkv"]), "bqkv": a["L0_attn_bqkv"],
        "wout": chunked(a["L0_attn_Wout"]), "bout": a["L0_attn_bout"],
        "lqkv": chunked(np.concatenate([a["L1_attn_Wq"], a["L1_attn_Wk"], a["L1_attn_Wv"]]).T),
        "lbias": np.concatenate([a["L1_attn_bq"], a["L1_attn_bk"], a["L1_attn_bv"]]),
        "lout": chunked(a["L1_attn_Wo"].T), "lbout": a["L1_attn_bo"], "rand": c(a["L1_attn_rand_matrix"].T),
        "w1": chunked(a["L1_ffn_W1"].T), "w3": chunked(a["L1_ffn_W3"].T), "w2": chunked(a["L1_ffn_W2"].T),
        "ident": np.eye(P, dtype=np.float32), "had": c(np.stack([had, -had], axis=1)),
        "iota": np.broadcast_to(np.arange(E, dtype=np.float32), (P, E)).copy(),
        "rope_c": tiled(np.concatenate([cos, cos], axis=1)), "rope_s": tiled(np.concatenate([-sin, sin], axis=1)),
        "rope_c16": sixteens(np.concatenate([cos, cos], axis=1)),
        "rope_s16": sixteens(np.concatenate([-sin, sin], axis=1)), "mask": mask,
    }


def kernel(**inputs):
    import numpy as _np
    import concourse.bacc as _bacc
    from concourse import mybir as _mybir
    from concourse.bass_utils import run_bass_kernel_spmd as _run

    nc = _bacc.Bacc("TRN2", target_bir_lowering=False, num_devices=1)
    laid = _laid_out({n: _np.asarray(v) for n, v in inputs.items()})
    arrays, ins = {}, {}
    for name, a in laid.items():
        arrays[f"in_{name}"] = _np.ascontiguousarray(a)
        ins[name] = nc.dram_tensor(f"in_{name}", a.shape, _mybir.dt.from_np(a.dtype), kind="ExternalInput").ap()
    out = nc.dram_tensor("out_x", (BATCH, SEQ, D), F32, kind="ExternalOutput").ap()
    program(nc, ins, out)
    r = _run(nc, [arrays], core_ids=[0])
    return r.results[0]["out_x"]
```
